# Optimizing a Trainium2 kernel written in Bass

```python
import numpy as np
import jax
import jax.numpy as jnp

def _softmax(x, axis=-1):
    return jax.nn.softmax(x, axis=axis)

def _gelu(x):
    return jax.nn.gelu(x, approximate=True)

def _silu(x):
    return jax.nn.silu(x)

def _sigmoid(x):
    return jax.nn.sigmoid(x)

def _layernorm(x, axis=-1, eps=1e-05):
    m = jnp.mean(x, axis=axis, keepdims=True)
    v = jnp.var(x, axis=axis, keepdims=True)
    return (x - m) / jnp.sqrt(v + eps)

def _scatter_add(tgt, idx, src, axis=0):
    return tgt.at[idx].add(src)

def _segment_sum(src, seg, n):
    return jax.ops.segment_sum(src, seg, n)
kernel_name = 'mk_macaron_d1_jaxref_r8_458851'

def setup_inputs(seed: int=0):
    np.random.seed(seed)
    _w = jnp.asarray

    def _L0_attn_setup():
        import jax, jax.numpy as jnp
        import numpy as np
        from jax import lax
        H, P, N, G, K, CHUNK = (64, 64, 128, 1, 4, 32)
        D_MODEL = 256
        D_INNER = H * P
        CONV_DIM = D_INNER + 2 * G * N
        EPS = 1e-05

        def _mamba2_forward(hidden_states, in_proj_w, conv_w, conv_b, dt_bias, A_log, D_param, norm_w, out_proj_w):
            b, l, _ = hidden_states.shape
            c = l // CHUNK
            proj = hidden_states @ in_proj_w
            gate = proj[..., :D_INNER]
            hbc = proj[..., D_INNER:D_INNER + CONV_DIM]
            dt = proj[..., D_INNER + CONV_DIM:]
            xt = hbc.transpose(0, 2, 1)
            y = lax.conv_general_dilated(xt, conv_w[:, None, :], window_strides=(1,), padding=[(K - 1, 0)], feature_group_count=CONV_DIM, dimension_numbers=('NCH', 'OIH', 'NCH'))
            hbc = jax.nn.silu(y + conv_b[None, :, None]).transpose(0, 2, 1)
            per_g = D_INNER // G
            hg = hbc.reshape(b, l, G, per_g + 2 * N)
            x = hg[..., :per_g].reshape(b, l, H, P)
            Bm = hg[..., per_g:per_g + N]
            Cm = hg[..., per_g + N:]
            hpg = H // G
            Bh = jnp.repeat(Bm, hpg, axis=2)
            Ch = jnp.repeat(Cm, hpg, axis=2)
            dt = jax.nn.softplus(dt + dt_bias)
            A = -jnp.exp(A_log)
            x_c = x.reshape(b, c, CHUNK, H, P)
            B_c = Bh.reshape(b, c, CHUNK, H, N)
            C_c = Ch.reshape(b, c, CHUNK, H, N)
            dt_c = dt.reshape(b, c, CHUNK, H)
            dA = dt_c * A[None, None, None, :]
            cum = jnp.cumsum(dA, axis=2)
            diff = cum[:, :, :, None, :] - cum[:, :, None, :, :]
            i = jnp.arange(CHUNK)
            mask = i[:, None] >= i[None, :]
            decay = jnp.exp(jnp.where(mask[None, None, :, :, None], diff, -jnp.inf))
            scores = jnp.einsum('bcihn,bcjhn->bcijh', C_c, B_c) * decay * dt_c[:, :, None, :, :]
            Y_diag = jnp.einsum('bcijh,bcjhp->bcihp', scores, x_c)
            decay_states = jnp.exp(cum[:, :, -1:, :] - cum)
            states = jnp.einsum('bclh,bclhn,bclhp->bchpn', decay_states * dt_c, B_c, x_c)
            chunk_decay = jnp.exp(cum[:, :, -1, :])

            def step(prev, inp):
                st, cd = inp
                new = cd[:, :, None, None] * prev + st
                return (new, prev)
            init = jnp.zeros((b, H, P, N), hidden_states.dtype)
            _, prev_states = lax.scan(step, init, (jnp.moveaxis(states, 1, 0), jnp.moveaxis(chunk_decay, 1, 0)))
            prev_states = jnp.moveaxis(prev_states, 0, 1)
            state_decay_out = jnp.exp(cum)
            Y_off = jnp.einsum('bclhn,bchpn,bclh->bclhp', C_c, prev_states, state_decay_out)
            yh = (Y_diag + Y_off).reshape(b, l, H, P) + D_param[None, None, :, None] * x
            yr = yh.reshape(b, l, D_INNER)
            hidden = yr * jax.nn.silu(gate)
            var = jnp.mean(hidden * hidden, axis=-1, keepdims=True)
            hidden = hidden * lax.rsqrt(var + EPS) * norm_w
            return hidden @ out_proj_w
        key = jax.random.key(seed)
        ks = jax.random.split(key, 6)
        s = lambda k, shape, scale: jax.random.normal(k, shape, jnp.float32) * scale
        return {'hidden_states': s(ks[0], (2, 256, D_MODEL), 1.0), 'in_proj_w': s(ks[1], (D_MODEL, D_INNER + CONV_DIM + H), D_MODEL ** (-0.5)), 'conv_w': s(ks[2], (CONV_DIM, K), K ** (-0.5)), 'conv_b': jnp.zeros((CONV_DIM,), jnp.float32), 'dt_bias': jnp.ones((H,), jnp.float32), 'A_log': jnp.log(jnp.arange(1, H + 1, dtype=jnp.float32)), 'D_param': jnp.ones((H,), jnp.float32), 'norm_w': jnp.ones((D_INNER,), jnp.float32), 'out_proj_w': s(ks[3], (D_INNER, D_MODEL), D_INNER ** (-0.5))}
    _L0_attn_in = _L0_attn_setup()

    def _L0_ffn_setup():
        import jax, jax.numpy as jnp
        import numpy as np
        HIDDEN = 256
        INTER = 688
        LUT_SIZE = 16

        def _ghost_linear(x, idx, lut):
            w = lut[idx]
            return jnp.einsum('bsh,oh->bso', x, w)
        key = jax.random.key(seed)
        k_x, k_lut, k_g, k_u, k_d = jax.random.split(key, 5)
        x = jax.random.normal(k_x, (2, 512, HIDDEN), dtype=jnp.float32)
        lut = jax.random.normal(k_lut, (LUT_SIZE,), dtype=jnp.float32) * 0.02
        gate_idx = jax.random.randint(k_g, (INTER, HIDDEN), 0, LUT_SIZE, dtype=jnp.int32)
        up_idx = jax.random.randint(k_u, (INTER, HIDDEN), 0, LUT_SIZE, dtype=jnp.int32)
        down_idx = jax.random.randint(k_d, (HIDDEN, INTER), 0, LUT_SIZE, dtype=jnp.int32)
        return {'x': x, 'lut': lut, 'gate_idx': gate_idx, 'up_idx': up_idx, 'down_idx': down_idx}
    _L0_ffn_in = _L0_ffn_setup()
    _d = {'L0_attn_hidden_states': _L0_attn_in['hidden_states'], 'L0_attn_in_proj_w': _L0_attn_in['in_proj_w'], 'L0_attn_conv_w': _L0_attn_in['conv_w'], 'L0_attn_conv_b': _L0_attn_in['conv_b'], 'L0_attn_dt_bias': _L0_attn_in['dt_bias'], 'L0_attn_A_log': _L0_attn_in['A_log'], 'L0_attn_D_param': _L0_attn_in['D_param'], 'L0_attn_norm_w': _L0_attn_in['norm_w'], 'L0_attn_out_proj_w': _L0_attn_in['out_proj_w'], 'L0_ffn_lut': _L0_ffn_in['lut'], 'L0_ffn_gate_idx': _L0_ffn_in['gate_idx'], 'L0_ffn_up_idx': _L0_ffn_in['up_idx'], 'L0_ffn_down_idx': _L0_ffn_in['down_idx']}
    _x0 = _d['L0_attn_hidden_states']
    _d['L0_attn_hidden_states'] = jax.random.normal(jax.random.fold_in(jax.random.key(seed), 1), (1, 2048, 256), dtype=_x0.dtype)
    del _x0
    return _d

def reference(L0_attn_hidden_states, L0_attn_in_proj_w, L0_attn_conv_w, L0_attn_conv_b, L0_attn_dt_bias, L0_attn_A_log, L0_attn_D_param, L0_attn_norm_w, L0_attn_out_proj_w, L0_ffn_lut, L0_ffn_gate_idx, L0_ffn_up_idx, L0_ffn_down_idx):

    def _L0_attn_ref(hidden_states, in_proj_w, conv_w, conv_b, dt_bias, A_log, D_param, norm_w, out_proj_w):
        import jax, jax.numpy as jnp
        import numpy as np
        from jax import lax
        H, P, N, G, K, CHUNK = (64, 64, 128, 1, 4, 32)
        D_MODEL = 256
        D_INNER = H * P
        CONV_DIM = D_INNER + 2 * G * N
        EPS = 1e-05

        def _mamba2_forward(hidden_states, in_proj_w, conv_w, conv_b, dt_bias, A_log, D_param, norm_w, out_proj_w):
            b, l, _ = hidden_states.shape
            c = l // CHUNK
            proj = hidden_states @ in_proj_w
            gate = proj[..., :D_INNER]
            hbc = proj[..., D_INNER:D_INNER + CONV_DIM]
            dt = proj[..., D_INNER + CONV_DIM:]
            xt = hbc.transpose(0, 2, 1)
            y = lax.conv_general_dilated(xt, conv_w[:, None, :], window_strides=(1,), padding=[(K - 1, 0)], feature_group_count=CONV_DIM, dimension_numbers=('NCH', 'OIH', 'NCH'))
            hbc = jax.nn.silu(y + conv_b[None, :, None]).transpose(0, 2, 1)
            per_g = D_INNER // G
            hg = hbc.reshape(b, l, G, per_g + 2 * N)
            x = hg[..., :per_g].reshape(b, l, H, P)
            Bm = hg[..., per_g:per_g + N]
            Cm = hg[..., per_g + N:]
            hpg = H // G
            Bh = jnp.repeat(Bm, hpg, axis=2)
            Ch = jnp.repeat(Cm, hpg, axis=2)
            dt = jax.nn.softplus(dt + dt_bias)
            A = -jnp.exp(A_log)
            x_c = x.reshape(b, c, CHUNK, H, P)
            B_c = Bh.reshape(b, c, CHUNK, H, N)
            C_c = Ch.reshape(b, c, CHUNK, H, N)
            dt_c = dt.reshape(b, c, CHUNK, H)
            dA = dt_c * A[None, None, None, :]
            cum = jnp.cumsum(dA, axis=2)
            diff = cum[:, :, :, None, :] - cum[:, :, None, :, :]
            i = jnp.arange(CHUNK)
            mask = i[:, None] >= i[None, :]
            decay = jnp.exp(jnp.where(mask[None, None, :, :, None], diff, -jnp.inf))
            scores = jnp.einsum('bcihn,bcjhn->bcijh', C_c, B_c) * decay * dt_c[:, :, None, :, :]
            Y_diag = jnp.einsum('bcijh,bcjhp->bcihp', scores, x_c)
            decay_states = jnp.exp(cum[:, :, -1:, :] - cum)
            states = jnp.einsum('bclh,bclhn,bclhp->bchpn', decay_states * dt_c, B_c, x_c)
            chunk_decay = jnp.exp(cum[:, :, -1, :])

            def step(prev, inp):
                st, cd = inp
                new = cd[:, :, None, None] * prev + st
                return (new, prev)
            init = jnp.zeros((b, H, P, N), hidden_states.dtype)
            _, prev_states = lax.scan(step, init, (jnp.moveaxis(states, 1, 0), jnp.moveaxis(chunk_decay, 1, 0)))
            prev_states = jnp.moveaxis(prev_states, 0, 1)
            state_decay_out = jnp.exp(cum)
            Y_off = jnp.einsum('bclhn,bchpn,bclh->bclhp', C_c, prev_states, state_decay_out)
            yh = (Y_diag + Y_off).reshape(b, l, H, P) + D_param[None, None, :, None] * x
            yr = yh.reshape(b, l, D_INNER)
            hidden = yr * jax.nn.silu(gate)
            var = jnp.mean(hidden * hidden, axis=-1, keepdims=True)
            hidden = hidden * lax.rsqrt(var + EPS) * norm_w
            return hidden @ out_proj_w
        return _mamba2_forward(hidden_states, in_proj_w, conv_w, conv_b, dt_bias, A_log, D_param, norm_w, out_proj_w)

    def _L0_ffn_ref(x, lut, gate_idx, up_idx, down_idx):
        import jax, jax.numpy as jnp
        import numpy as np
        HIDDEN = 256
        INTER = 688
        LUT_SIZE = 16

        def _ghost_linear(x, idx, lut):
            w = lut[idx]
            return jnp.einsum('bsh,oh->bso', x, w)
        gate = _ghost_linear(x, gate_idx, lut)
        up = _ghost_linear(x, up_idx, lut)
        h = jax.nn.silu(gate) * up
        return _ghost_linear(h, down_idx, lut)
    x = L0_attn_hidden_states
    x = x + 0.5 * _L0_ffn_ref(_layernorm(x, axis=-1), L0_ffn_lut, L0_ffn_gate_idx, L0_ffn_up_idx, L0_ffn_down_idx)
    x = x + _L0_attn_ref(_layernorm(x, axis=-1), L0_attn_in_proj_w, L0_attn_conv_w, L0_attn_conv_b, L0_attn_dt_bias, L0_attn_A_log, L0_attn_D_param, L0_attn_norm_w, L0_attn_out_proj_w)
    x = x + 0.5 * _L0_ffn_ref(_layernorm(x, axis=-1), L0_ffn_lut, L0_ffn_gate_idx, L0_ffn_up_idx, L0_ffn_down_idx)
    return x

_drawn_inputs = setup_inputs


def setup_inputs(seed=0):
    import zlib

    import numpy as np

    out = dict(_drawn_inputs(seed))
    spreads = {'L0_attn_conv_b': (0.0, 0.1),
     'L0_attn_dt_bias': (1.0, 0.2),
     'L0_attn_D_param': (1.0, 0.2),
     'L0_attn_norm_w': (1.0, 0.2)}
    factors = {}
    for name, (base, spread) in spreads.items():
        noise = np.random.default_rng([zlib.crc32(name.encode()), seed]).standard_normal(out[name].shape)
        drawn = base * np.exp(spread * noise) if base else spread * noise
        out[name] = jnp.asarray(drawn.astype(out[name].dtype))
    for name, factor in factors.items():
        out[name] = (out[name] * factor).astype(out[name].dtype)
    return out
```

```python
from contextlib import ExitStack

import concourse.bass as bass
from concourse import mybir

F32 = mybir.dt.float32
F32R = mybir.dt.float32r
I32 = mybir.dt.int32
ALU = mybir.AluOpType
ACT = mybir.ActivationFunctionType

P = 128
L = 2048
D = 256
KT = D // P
INTER = 688
MT = -(-INTER // P)
LUT = 16
H, HP, N = 64, 64, 128
DI = H * HP
TT = 512
NT = L // TT
CH = P
NC = L // CH
CPT = TT // CH
PAIRS = H // 2
TAPS = 4
EPS = 1e-5


def split_matmul(nc, out, l_hi, l_lo, r_hi, r_lo, start, stop, skip=False):
    nc.tensor.matmul(out, l_hi, r_hi, start=start, stop=False, skip_group_check=skip)
    nc.tensor.matmul(out, l_hi, r_lo, start=False, stop=False, skip_group_check=skip)
    return nc.tensor.matmul(out, l_lo, r_hi, start=False, stop=stop, skip_group_check=skip)


class LayerNorm:

    def __init__(self, nc, name, sem, sb, x_res, xn, xT_hi, xT_lo, banks, ident):
        self.nc, self.x, self.xn, self.hi, self.lo, self.banks, self.ident = nc, x_res, xn, xT_hi, xT_lo, banks, ident
        self.stats = sb(name + "_stats", [P, NC, 6], F32)
        self.mv = sb(name + "_mv", [P, NC, 2], F32)
        self.ve = sb(name + "_ve", [P, NC], F32)
        self.sd = sb(name + "_sd", [P, NC], F32)
        self.rstd = sb(name + "_rstd", [P, NC], F32)
        self.t = sb(name + "_t", [P, NC], F32)
        self.step = sem(name + "_vector_step")
        self.steps = 0
        self.var_ready = sem(name + "_var_ready")
        self.sd_ready = sem(name + "_sd_ready")
        self.norm_done = sem(name + "_norm_done")
        self.transposed = sem(name + "_transposed")
        self.hi_done = sem(name + "_hi_done")
        self.lo_done = sem(name + "_lo_done")

    def chain(self, dve, ins):
        self.steps += 1
        ins.then_inc(self.step, 1)
        dve.wait_ge(self.step, self.steps)

    def stats_of(self, s):
        self.nc.vector.bn_stats(self.stats[:, s, :], self.x[:, s, :]).then_inc(self.step, 1)
        self.steps += 1

    def vector_stats(self, dve):
        nc = self.nc
        dve.wait_ge(self.step, self.steps)
        for s in range(NC):
            last = nc.vector.bn_aggr(self.mv[:, s, :], self.stats[:, s, :])
        self.chain(dve, last)
        nc.vector.tensor_scalar(self.ve[:], self.mv[:, :, 1], EPS, None, ALU.add).then_inc(self.var_ready, 1)

    def vector_normalise(self, dve):
        rsqrt_from_sqrt(self.nc, dve, self.sd, self.ve, self.rstd, self.t, self.sd_ready, self.chain)
        for s in range(NC):
            self.nc.vector.tensor_scalar(self.xn[:, s, :], self.x[:, s, :], self.mv[:, s, 0:1],
                                         self.rstd[:, s:s + 1], ALU.subtract, ALU.mult).then_inc(self.norm_done, 1)

    def scalar_sqrt(self, act):
        act.wait_ge(self.var_ready, 1)
        self.nc.scalar.activation(self.sd[:], self.ve[:], ACT.Sqrt).then_inc(self.sd_ready, 1)

    def tensor_transpose(self, pe):
        nc, rings = self.nc, len(self.banks)
        for g in range(NT):
            if g >= rings:
                pe.wait_ge(self.lo_done, KT * (g - rings + 1))
            for s in range(CPT * g, CPT * g + CPT):
                pe.wait_ge(self.norm_done, s + 1)
                for kt in range(KT):
                    c = (s % CPT) * P
                    last = nc.tensor.transpose(self.banks[g % rings][kt][:, c:c + P],
                                               self.xn[:, s, kt * P:(kt + 1) * P], self.ident[:])
            last.then_inc(self.transposed, 1)

    def scalar_hi(self, act):
        for g in range(NT):
            act.wait_ge(self.transposed, g + 1)
            for kt in range(KT):
                self.nc.scalar.activation(self.hi[:, kt, g * TT:(g + 1) * TT],
                                          self.banks[g % len(self.banks)][kt], ACT.Copy).then_inc(self.hi_done, 1)

    def vector_lo(self, dve):
        for g in range(NT):
            for kt in range(KT):
                dve.wait_ge(self.hi_done, KT * g + kt + 1)
                self.nc.vector.tensor_tensor(self.lo[:, kt, g * TT:(g + 1) * TT],
                                             self.banks[g % len(self.banks)][kt],
                                             self.hi[:, kt, g * TT:(g + 1) * TT].bitcast(F32),
                                             ALU.subtract).then_inc(self.lo_done, 1)


def rsqrt_from_sqrt(nc, dve, sd, ve, rstd, t, sd_ready, chain):
    dve.wait_ge(sd_ready, 1)
    chain(dve, nc.vector.reciprocal(rstd[:], sd[:]))
    chain(dve, nc.vector.tensor_tensor(t[:], rstd[:], rstd[:], ALU.mult))
    chain(dve, nc.vector.tensor_tensor(t[:], t[:], ve[:], ALU.mult))
    chain(dve, nc.vector.tensor_scalar(t[:], t[:], -0.5, 1.5, ALU.mult, ALU.add))
    chain(dve, nc.vector.tensor_tensor(rstd[:], rstd[:], t[:], ALU.mult))


class Ffn:

    def __init__(self, nc, name, sem, sb, bank, x_res, xT_hi, xT_lo, w):
        self.nc, self.x, self.xh, self.xl, self.w = nc, x_res, xT_hi, xT_lo, w
        self.gate = [bank(0), bank(1)]
        self.up = [bank(2), bank(3)]
        self.down = [bank(4), bank(5)]
        self.sg = sb(name + "_silu_gate", [P, 2, TT], F32)
        self.h = sb(name + "_hidden", [P, 3, TT], F32)
        self.hh = sb(name + "_hidden_hi", [P, MT, TT], F32R)
        self.hl = sb(name + "_hidden_lo", [P, MT, TT], F32R)
        self.gate_done = sem(name + "_gate_done")
        self.up_done = sem(name + "_up_done")
        self.silu_done = sem(name + "_silu_done")
        self.h_done = sem(name + "_h_done")
        self.hi_done = sem(name + "_hi_done")
        self.lo_done = sem(name + "_lo_done")
        self.slot_free = sem(name + "_slot_free")
        self.tile_done = sem(name + "_tile_done")
        self.x_done = sem(name + "_x_done")

    def tensor(self, pe, before):
        nc = self.nc
        before()

        def down(T, m):
            pe.wait_ge(self.lo_done, T * MT + m + 2)
            if m == 0:
                pe.wait_ge(self.x_done, T + 1)
            for s in range(CPT):
                out = self.down[s // 2][:, (s % 2) * D:(s % 2 + 1) * D]
                last = split_matmul(nc, out, self.hh[:, m, s * P:(s + 1) * P], self.hl[:, m, s * P:(s + 1) * P],
                                    self.w["down_hi"][:, m, :], self.w["down_lo"][:, m, :],
                                    start=(m == 0 and s % 2 == 0), stop=(m == MT - 1), skip=True)
            last.then_inc(self.slot_free, 1)
            return last

        with pe.Fori(0, NT) as T:
            for m in range(MT):
                for what, banks, done, free in (("gate", self.gate, self.gate_done, self.silu_done),
                                                ("up", self.up, self.up_done, self.h_done)):
                    pe.wait_ge(free, T * MT + m + 1)
                    for kt in range(KT):
                        last = split_matmul(nc, banks[m % 2], self.w[what + "_hi"][:, kt, m * P:(m + 1) * P],
                                            self.w[what + "_lo"][:, kt, m * P:(m + 1) * P],
                                            self.xh[:, kt, bass.ds(T * TT, TT)], self.xl[:, kt, bass.ds(T * TT, TT)],
                                            start=(kt == 0), stop=(kt == KT - 1))
                    last.then_inc(done, 1)
                if m >= 2:
                    down(T, m - 2)
            down(T, MT - 2)
            down(T, MT - 1)

    def scalar(self, act):
        nc = self.nc
        act.sem_inc(self.silu_done, 2)

        def hi(T, m):
            act.wait_ge(self.h_done, T * MT + m + 3)
            act.wait_ge(self.slot_free, T * MT + m + 1)
            nc.scalar.activation(self.hh[:, m, :], self.h[:, m % 3, :], ACT.Copy).then_inc(self.hi_done, 1)

        with act.Fori(0, NT) as T:
            for m in range(MT):
                act.wait_ge(self.gate_done, T * MT + m + 1)
                act.wait_ge(self.h_done, T * MT + m + 1)
                nc.scalar.activation(self.sg[:, m % 2, :], self.gate[m % 2], ACT.Silu).then_inc(self.silu_done, 1)
                if m >= 1:
                    hi(T, m - 1)
            hi(T, MT - 1)

    def vector(self, dve):
        nc = self.nc
        dve.sem_inc(self.h_done, 2)

        def lo(T, m):
            dve.wait_ge(self.hi_done, T * MT + m + 1)
            nc.vector.tensor_tensor(self.hl[:, m, :], self.h[:, m % 3, :], self.hh[:, m, :].bitcast(F32),
                                    ALU.subtract).then_inc(self.lo_done, 1)

        with dve.Fori(0, NT) as T:
            for m in range(MT):
                dve.wait_ge(self.silu_done, T * MT + m + 3)
                dve.wait_ge(self.up_done, T * MT + m + 1)
                dve.wait_ge(self.lo_done, T * MT + max(m - 2, 0) + 1)
                nc.vector.tensor_tensor(self.h[:, m % 3, :], self.up[m % 2], self.sg[:, m % 2, :],
                                        ALU.mult).then_inc(self.h_done, 1)
                if m >= 1:
                    lo(T, m - 1)
            lo(T, MT - 1)
            dve.wait_ge(self.slot_free, T * MT + MT + MT)
            for b in range(2):
                xs = self.x[:, bass.ds(T * CPT + 2 * b, 2), :]
                last = nc.vector.scalar_tensor_tensor(xs, self.down[b].rearrange("p (s d) -> p s d", s=2), 0.5, xs,
                                                      ALU.mult, ALU.add)
            last.then_inc(self.x_done, 1)

    def pool(self, pool):
        pool.sem_inc(self.slot_free, MT)
        pool.sem_inc(self.lo_done, 1)
        pool.sem_inc(self.x_done, 1)


def macaron(nc, x, w_in, conv_w, conv_b, dt_bias, a_log, d_param, norm_w, w_out, lut, gate_idx, up_idx, down_idx, out):
    x_rows = x[0].rearrange("(s p) d -> p s d", p=P)
    out_rows = out[0].rearrange("(s p) d -> p s d", p=P)
    w_in_t = w_in.rearrange("(kt p) n -> p kt n", p=P)
    X_COL, B_COL, DT_COL = DI, 2 * DI, 2 * DI + 2 * N

    ctx = ExitStack()
    sem = lambda name: ctx.enter_context(nc.semaphore(name))

    def scope():
        stack = ExitStack()
        return stack, (lambda name, shape, dt: stack.enter_context(nc.sbuf_tensor(name, shape, dt)))

    x1_dram = nc.dram_tensor("x1_scratch", (P, NC, D), F32, kind="Internal").ap()
    cum_dram = nc.dram_tensor("cum_scratch", (H, L), F32, kind="Internal").ap()
    ffn_w_shapes = {"gate": [P, KT, MT * P], "up": [P, KT, MT * P], "down": [P, MT, D]}
    w_dram = {n + part: nc.dram_tensor(n + part + "_scratch", tuple(shape), F32, kind="Internal").ap()
              for n, shape in ffn_w_shapes.items() for part in ("_hi", "_lo")}

    psum = ctx.enter_context(nc.psum_tensor("psum", [P, 8, TT], F32))
    bank = lambda b: psum[:, b, :]

    whole, sbw = scope()
    ident = sbw("ident", [P, P], F32)
    upper = sbw("upper", [P, P], F32)
    ones = sbw("ones", [P, P], F32)
    xT_hi = sbw("xT_hi", [P, KT, L], F32R)
    xT_lo = sbw("xT_lo", [P, KT, L], F32R)

    PART = NC * 2
    CUM, DT, E_CUM, TO_END, CHUNK_DECAY = range(0, 5 * PART, PART)
    D_AT, NORM_AT, CONV_AT = 5 * PART, 5 * PART + 1, 5 * PART + 2
    BIAS_AT = CONV_AT + TAPS
    HEAD = 1
    ROW = HEAD + BIAS_AT + 1
    table_dram = nc.dram_tensor("table_scratch", (P, PAIRS, ROW), F32, kind="Internal").ap()

    st, sb = scope()
    x_res = sb("x_res1", [P, NC, D], F32)
    xn = sb("xn1", [P, NC, D], F32)
    w = {n + part: sb(n + part + "1", shape, F32R)
         for n, shape in ffn_w_shapes.items() for part in ("_hi", "_lo")}
    lut_sb = sb("lut_sb", [P, LUT], F32)
    idx = {"gate": sb("gate_idx_sb", [P, MT, D], I32), "up": sb("up_idx_sb", [P, MT, D], I32),
           "down": sb("down_idx_sb", [P, KT, MT * P], I32)}
    picked = sb("picked", [P, 2, MT * D], F32)
    ln1 = LayerNorm(nc, "ln1", sem, sb, x_res, xn, xT_hi, xT_lo, [(bank(6), bank(7))], ident)
    ffn1 = Ffn(nc, "ffn1", sem, sb, bank, x_res, xT_hi, xT_lo, w)
    ln2 = LayerNorm(nc, "ln2", sem, sb, x_res, xn, xT_hi, xT_lo, [(bank(6), bank(7)), (bank(4), bank(5))], ident)
    x_in = [sem(f"x_in{g}") for g in range(NT)]
    lut_in = sem("lut_in")
    idx_in = {n: sem(n + "_idx_in") for n in idx}
    pad_done = sem("pad_done")
    const_done = sem("const_done")
    picked_done = sem("picked_done")
    picked_used = sem("picked_used")
    decoded = sem("decoded")
    w_hi_done = sem("w_hi_done")
    w_lo_done = sem("w_lo_done")
    spilled = sem("spilled")
    ORDER = ("gate", "up", "down")
    dec_bank = {"gate": 0, "up": 3, "down": 0}

    def dec_psum(n):
        return psum[:, dec_bank[n]:dec_bank[n] + 3, :].rearrange("p b c -> p (b c)")

    with nc.Block() as block:
        @block.sync
        def _(sp):
            sp.dma_start(lut_sb[:], lut.partition_broadcast(P)).then_inc(lut_in, 16)
            sp.wait_ge(pad_done, 3)
            full = INTER // P
            for n, src in (("gate", gate_idx), ("up", up_idx)):
                sp.dma_start(idx[n][:, 0:full, :],
                             src[0:full * P, :].rearrange("(t p) d -> p t d", p=P)).then_inc(idx_in[n], 16)
                sp.dma_start(idx[n][0:INTER - full * P, full, :], src[full * P:INTER, :]).then_inc(idx_in[n], 16)
            sp.dma_start(idx["down"][:, :, 0:INTER],
                         down_idx.rearrange("(t p) d -> p t d", p=P)).then_inc(idx_in["down"], 16)
            for i, n in enumerate(ORDER):
                sp.wait_ge(w_hi_done, i + 1)
                sp.wait_ge(w_lo_done, i + 1)
                for part in ("_hi", "_lo"):
                    sp.dma_start(w_dram[n + part], w[n + part][:].bitcast(F32)).then_inc(spilled, 16)
            sp.wait_ge(ffn1.x_done, NT + 1)
            sp.dma_start(x1_dram, x_res[:]).then_inc(spilled, 16)
            sp.wait_ge(spilled, 16 * (2 * len(ORDER) + 1))

        @block.gpsimd
        def _(pool):
            nc.gpsimd.memset(idx["gate"][:, MT - 1, :], -1).then_inc(pad_done, 1)
            nc.gpsimd.memset(idx["up"][:, MT - 1, :], -1).then_inc(pad_done, 1)
            nc.gpsimd.memset(idx["down"][:, :, INTER:], -1).then_inc(pad_done, 1)
            nc.gpsimd.memset(ident[:], 0.0).then_inc(const_done, 1)
            nc.gpsimd.memset(upper[:], 1.0).then_inc(const_done, 1)
            nc.gpsimd.memset(ones[:], 1.0).then_inc(const_done, 1)
            pool.wait_ge(const_done, 3)
            nc.gpsimd.affine_select(out=ident[:], in_=ident[:], compare_op=ALU.not_equal, fill=1.0, base=0,
                                    pattern=[[-1, P]], channel_multiplier=1).then_inc(const_done, 1)
            nc.gpsimd.affine_select(out=upper[:], in_=upper[:], compare_op=ALU.is_ge, fill=0.0, base=0,
                                    pattern=[[1, P]], channel_multiplier=-1).then_inc(const_done, 1)
            ffn1.pool(pool)

        @block.scalar
        def _(act):
            for g in range(NT):
                act.dma_start(x_res[:, g * CPT:(g + 1) * CPT, :],
                              x_rows[:, g * CPT:(g + 1) * CPT, :]).then_inc(x_in[g], 16)
            ln1.scalar_sqrt(act)
            ln1.scalar_hi(act)
            for i, n in enumerate(ORDER):
                act.wait_ge(decoded, i + 1)
                nc.scalar.activation(w[n + "_hi"][:].rearrange("p a b -> p (a b)"), dec_psum(n),
                                     ACT.Copy).then_inc(w_hi_done, 1)
            ffn1.scalar(act)
            ln2.scalar_sqrt(act)
            ln2.scalar_hi(act)

        @block.vector
        def _(dve):
            for s in range(NC):
                if s % CPT == 0:
                    dve.wait_ge(x_in[s // CPT], 16)
                ln1.stats_of(s)
            ln1.vector_stats(dve)
            ln1.vector_normalise(dve)
            ln1.vector_lo(dve)

            def pick(i, n):
                dve.wait_ge(idx_in[n], 32 if n != "down" else 16)
                for k in range(LUT):
                    step = i * LUT + k
                    if step >= 2:
                        dve.wait_ge(picked_used, step - 1)
                    nc.vector.tensor_scalar(picked[:, step % 2, :], idx[n][:].rearrange("p a b -> p (a b)"), float(k),
                                            lut_sb[:, k:k + 1], ALU.is_equal, ALU.mult).then_inc(picked_done, 1)

            def weights_lo(i, n):
                dve.wait_ge(w_hi_done, i + 1)
                nc.vector.tensor_tensor(w[n + "_lo"][:].rearrange("p a b -> p (a b)"), dec_psum(n),
                                        w[n + "_hi"][:].rearrange("p a b -> p (a b)").bitcast(F32),
                                        ALU.subtract).then_inc(w_lo_done, 1)

            dve.wait_ge(lut_in, 16)
            pick(0, "gate")
            pick(1, "up")
            weights_lo(0, "gate")
            pick(2, "down")
            weights_lo(1, "up")
            weights_lo(2, "down")
            ffn1.vector(dve)
            dve.wait_ge(ffn1.x_done, NT + 1)
            for s in range(NC):
                ln2.stats_of(s)
            ln2.vector_stats(dve)
            ln2.vector_normalise(dve)
            ln2.vector_lo(dve)

        @block.tensor
        def _(pe):
            pe.wait_ge(const_done, 5)
            ln1.tensor_transpose(pe)
            for i, n in enumerate(ORDER):
                if n == "down":
                    pe.wait_ge(w_lo_done, 1)
                rows, cols = idx[n].shape[1], idx[n].shape[2] // P
                for k in range(LUT):
                    step = i * LUT + k
                    pe.wait_ge(picked_done, step + 1)
                    for c in range(cols):
                        for r in range(rows):
                            block_at = c * rows + r
                            src = picked[:, step % 2, (r * cols + c) * P:(r * cols + c + 1) * P]
                            last = nc.tensor.matmul(dec_psum(n)[:, block_at * P:(block_at + 1) * P], src, ident[:],
                                                    start=(k == 0 and block_at % 4 == 0), stop=(k == LUT - 1),
                                                    is_transpose=True, skip_group_check=True)
                    last.then_inc(picked_used, 1)
                pe.wait_ge(picked_used, (i + 1) * LUT)
                pe.sem_inc(decoded, 1)
            ffn1.tensor(pe, lambda: pe.wait_ge(w_lo_done, 3))
            ln2.tensor_transpose(pe)
    st.close()

    acc_scope, sb = scope()
    mixed = sb("mixed", [P, KT, L], F32)
    squares = sb("squares", [P, L], F32)
    shared_scope, sb = scope()
    CT = sb("CT", [P, L], F32)
    B_tok = sb("B_tok", [P, NC, N], F32)
    CB = sb("CB", [P, NC, CH], F32)

    st, sb = scope()
    table = sb("table", [P, PAIRS, ROW], F32)
    dt = sb("dt", [P, NC, H], F32)
    w_bc_raw = sb("w_bc_raw", [P, KT, 2 * N], F32)
    w_bc_hi = sb("w_bc_hi", [P, KT, 2 * N], F32R)
    w_bc_lo = sb("w_bc_lo", [P, KT, 2 * N], F32R)
    w_dt_raw = sb("w_dt_raw", [P, KT, H], F32)
    w_dt_hi = sb("w_dt_hi", [P, KT, H], F32R)
    w_dt_lo = sb("w_dt_lo", [P, KT, H], F32R)
    conv_bc = sb("conv_bc", [P, 2, TAPS], F32)
    bias_bc = sb("bias_bc", [P, 2], F32)
    dt_bias_sb = sb("dt_bias_sb", [P, H], F32)
    a_exp = sb("a_exp", [P, H], F32)
    raw = sb("bc_raw", [P, 2, TAPS - 1 + L], F32)
    conv = sb("bc_conv", [P, 2, L], F32)
    z = sb("z", [P, NC, H], F32)
    zmax = sb("zmax", [P, NC, H], F32)
    ez = sb("ez", [P, NC, H], F32)
    ez1 = sb("ez1", [P, NC, H], F32)
    lnz = sb("lnz", [P, NC, H], F32)
    dA = sb("dA", [P, NC, H], F32)
    cum = sb("cum", [P, NC, H], F32)
    end_arg = sb("end_arg", [P, NC, H], F32)
    cumT = sb("cumT", [H, L], F32)

    w_small_in, conv_in, vec_in, chan_in = sem("w_small_in"), sem("conv_in"), sem("vec_in"), sem("chan_in")
    cum_out = sem("cum_out")
    raw_pad = sem("raw_pad")
    w_small_hi, w_small_lo = sem("w_small_hi"), sem("w_small_lo")
    bc_proj, bc_evac, bc_step, bc_ready = sem("bc_proj"), sem("bc_evac"), sem("bc_step"), sem("bc_ready")
    dt_proj, prep_step, a_ready = sem("dt_proj"), sem("prep_step"), sem("a_ready")
    na_ready, ez_ready, ez1_ready, ln_ready = sem("na_ready"), sem("ez_ready"), sem("ez1_ready"), sem("ln_ready")
    dA_ready, cum_psum, total_psum = sem("dA_ready"), sem("cum_psum"), sem("total_psum")
    cum_ready, end_arg_ready, decays_done = sem("cum_ready"), sem("end_arg_ready"), sem("decays_done")
    B_turned, B_tok_done, CB_psum, CB_done = sem("B_turned"), sem("B_tok_done"), sem("CB_psum"), sem("CB_done")
    cum_turned, cumT_done, dt_stored = sem("cum_turned"), sem("cumT_done"), sem("dt_stored")

    def part(at):
        return table[:, :, HEAD + at:HEAD + at + PART].rearrange("p k (c h) -> p c k h", h=2)

    by_pair = lambda t: t.rearrange("p c (k h) -> p c k h", h=2)

    two_banks = lambda b: psum[:, b:b + 2, :].rearrange("p b (c h) -> p (b c) h", h=H)

    with nc.Block() as block:
        @block.sync
        def _(sp):
            sp.dma_start(w_bc_raw[:], w_in_t[:, :, B_COL:B_COL + 2 * N]).then_inc(w_small_in, 16)
            sp.dma_start(w_dt_raw[:], w_in_t[:, :, DT_COL:DT_COL + H]).then_inc(w_small_in, 16)
            sp.dma_start(dt_bias_sb[:], dt_bias.partition_broadcast(P)).then_inc(vec_in, 16)
            sp.dma_start(a_exp[:], a_log.partition_broadcast(P)).then_inc(vec_in, 16)
            with nc.allow_non_contiguous_dma(reason="small per-channel vectors"):
                sp.dma_start(conv_bc[:], conv_w[DI:DI + 2 * N, :].rearrange("(k p) t -> p k t", p=P)).then_inc(conv_in, 16)
                sp.dma_start(bias_bc[:], conv_b[DI:DI + 2 * N].rearrange("(k p) -> p k", p=P)).then_inc(conv_in, 16)
                sp.dma_start(table[:, :, HEAD + CONV_AT:HEAD + BIAS_AT], conv_w[0:DI, :].rearrange("(k p) t -> p k t", p=P)).then_inc(chan_in, 16)
                sp.dma_start(table[:, :, HEAD + BIAS_AT], conv_b[0:DI].rearrange("(k p) -> p k", p=P)).then_inc(chan_in, 16)
                sp.dma_start(table[:, :, HEAD + NORM_AT], norm_w.rearrange("(k p) -> p k", p=P)).then_inc(chan_in, 16)
                d_pairs = d_param.rearrange("(k two) -> two k", two=2)
                for half in range(2):
                    sp.dma_start(table[half * HP:(half + 1) * HP, :, HEAD + D_AT],
                                 d_pairs[half].partition_broadcast(HP)).then_inc(chan_in, 16)
            sp.wait_ge(cumT_done, NT)
            sp.dma_start(cum_dram, cumT[:]).then_inc(cum_out, 16)
            sp.wait_ge(chan_in, 80)
            sp.wait_ge(decays_done, 4)
            sp.wait_ge(dt_stored, 2)
            sp.dma_start(table_dram, table[:]).then_inc(cum_out, 16)
            sp.wait_ge(cum_out, 32)

        @block.gpsimd
        def _(pool):
            nc.gpsimd.memset(raw[:, :, 0:TAPS - 1], 0.0).then_inc(raw_pad, 1)
            nc.gpsimd.memset(table[:, :, 0], 0.0).then_inc(dt_stored, 1)
            nc.gpsimd.memset(squares[:], 0.0)
            nc.gpsimd.memset(mixed[:], 0.0)

        @block.scalar
        def _(act):
            act.wait_ge(w_small_in, 32)
            nc.scalar.activation(w_bc_hi[:], w_bc_raw[:], ACT.Copy).then_inc(w_small_hi, 1)
            nc.scalar.activation(w_dt_hi[:], w_dt_raw[:], ACT.Copy).then_inc(w_small_hi, 1)
            act.wait_ge(vec_in, 32)
            nc.scalar.activation(a_exp[:], a_exp[:], ACT.Exp).then_inc(a_ready, 1)
            act.wait_ge(na_ready, 1)
            nc.scalar.activation(ez[:], ez[:], ACT.Exp).then_inc(ez_ready, 1)
            for g in range(2 * NT):
                act.wait_ge(bc_proj, g + 1)
                bc, t = divmod(g, NT)
                nc.scalar.activation(raw[:, bc, TAPS - 1 + t * TT:TAPS - 1 + (t + 1) * TT], bank(g % 4),
                                     ACT.Copy).then_inc(bc_evac, 1)
            act.wait_ge(ez1_ready, 1)
            nc.scalar.activation(lnz[:], ez1[:], ACT.Ln).then_inc(ln_ready, 1)
            act.wait_ge(cum_ready, 1)
            nc.scalar.activation(part(CUM), by_pair(cum[:]), ACT.Copy).then_inc(decays_done, 1)
            nc.scalar.activation(part(E_CUM), by_pair(cum[:]), ACT.Exp).then_inc(decays_done, 1)
            act.wait_ge(end_arg_ready, 1)
            nc.scalar.activation(part(CHUNK_DECAY), by_pair(two_banks(4)), ACT.Exp).then_inc(decays_done, 1)
            nc.scalar.activation(part(TO_END), by_pair(end_arg[:]), ACT.Exp).then_inc(decays_done, 1)
            act.wait_ge(bc_step, 2 * TAPS)
            nc.scalar.activation(conv[:, 0, :], conv[:, 0, :], ACT.Silu).then_inc(bc_ready, 1)
            nc.scalar.activation(CT[:], conv[:, 1, :], ACT.Silu).then_inc(bc_ready, 1)
            for g in range(NT):
                act.wait_ge(B_turned, g + 1)
                nc.scalar.activation(B_tok[:, g * CPT:(g + 1) * CPT, :],
                                     bank(g).rearrange("p (c n) -> p c n", n=N), ACT.Copy).then_inc(B_tok_done, 1)
            for g in range(NT):
                act.wait_ge(cum_turned, g + 1)
                nc.scalar.activation(cumT[:, g * TT:(g + 1) * TT], psum[0:H, 4 + g, :], ACT.Copy).then_inc(cumT_done, 1)

        @block.vector
        def _(dve):
            steps = [0]

            def chain(ins):
                steps[0] += 1
                ins.then_inc(prep_step, 1)
                dve.wait_ge(prep_step, steps[0])

            dve.wait_ge(w_small_hi, 2)
            nc.vector.tensor_tensor(w_bc_lo[:], w_bc_raw[:], w_bc_hi[:].bitcast(F32), ALU.subtract).then_inc(w_small_lo, 1)
            nc.vector.tensor_tensor(w_dt_lo[:], w_dt_raw[:], w_dt_hi[:].bitcast(F32), ALU.subtract).then_inc(w_small_lo, 1)
            dve.wait_ge(dt_proj, 1)
            dve.wait_ge(vec_in, 32)
            chain(nc.vector.tensor_tensor(z[:], two_banks(4), dt_bias_sb[:].unsqueeze(1).to_broadcast([P, NC, H]), ALU.add))
            chain(nc.vector.tensor_scalar(zmax[:], z[:], 0.0, None, ALU.max))
            nc.vector.scalar_tensor_tensor(ez[:], zmax[:], -2.0, z[:], ALU.mult, ALU.add).then_inc(na_ready, 1)
            dve.wait_ge(ez_ready, 1)
            nc.vector.tensor_scalar(ez1[:], ez[:], 1.0, None, ALU.add).then_inc(ez1_ready, 1)
            dve.wait_ge(ez1_ready, 1)
            chain(nc.vector.scalar_tensor_tensor(z[:], ez1[:], -1.0, ez[:], ALU.add, ALU.subtract))
            chain(nc.vector.tensor_tensor(zmax[:], zmax[:], z[:], ALU.subtract))
            dve.wait_ge(ln_ready, 1)
            chain(nc.vector.tensor_tensor(dt[:], lnz[:], zmax[:], ALU.add))
            dve.wait_ge(a_ready, 1)
            nc.vector.scalar_tensor_tensor(dA[:], dt[:], -1.0, a_exp[:].unsqueeze(1).to_broadcast([P, NC, H]),
                                           ALU.mult, ALU.mult).then_inc(dA_ready, 1)
            nc.vector.tensor_copy(part(DT), by_pair(dt[:])).then_inc(dt_stored, 1)
            dve.wait_ge(raw_pad, 1)
            dve.wait_ge(conv_in, 32)
            dve.wait_ge(bc_evac, 2 * NT)
            for tap in range(TAPS):
                for bc in range(2):
                    if tap == 0:
                        ins = nc.vector.tensor_scalar(conv[:, bc, :], raw[:, bc, 0:L], conv_bc[:, bc, 0:1],
                                                      bias_bc[:, bc:bc + 1], ALU.mult, ALU.add)
                    else:
                        dve.wait_ge(bc_step, 2 * (tap - 1) + bc + 1)
                        ins = nc.vector.scalar_tensor_tensor(conv[:, bc, :], raw[:, bc, tap:tap + L],
                                                             conv_bc[:, bc, tap:tap + 1], conv[:, bc, :],
                                                             ALU.mult, ALU.add)
                    ins.then_inc(bc_step, 1)
                if tap == 1:
                    dve.wait_ge(cum_psum, 1)
                    nc.vector.tensor_copy(cum[:], two_banks(6)).then_inc(cum_ready, 1)
                    dve.wait_ge(cum_ready, 1)
                    dve.wait_ge(total_psum, 1)
                    nc.vector.tensor_tensor(end_arg[:], two_banks(4), cum[:], ALU.subtract).then_inc(end_arg_ready, 1)
            for g in range(NT):
                dve.wait_ge(CB_psum, g + 1)
                nc.vector.tensor_tensor(CB[:, g * CPT:(g + 1) * CPT, :], bank(g).rearrange("p (c i) -> p c i", i=CH),
                                        upper[:].unsqueeze(1).to_broadcast([P, CPT, CH]), ALU.mult).then_inc(CB_done, 1)

        @block.tensor
        def _(pe):
            pe.wait_ge(w_small_lo, 2)
            for c in range(NC):
                out = two_banks(4)[:, c, :]
                for kt in range(KT):
                    last = split_matmul(nc, out, xT_hi[:, kt, c * CH:(c + 1) * CH], xT_lo[:, kt, c * CH:(c + 1) * CH],
                                        w_dt_hi[:, kt, :], w_dt_lo[:, kt, :], start=(kt == 0), stop=(kt == KT - 1))
            last.then_inc(dt_proj, 1)
            for g in range(2 * NT):
                bc, t = divmod(g, NT)
                if g >= 4:
                    pe.wait_ge(bc_evac, g - 3)
                for kt in range(KT):
                    last = split_matmul(nc, bank(g % 4), w_bc_hi[:, kt, bc * N:(bc + 1) * N],
                                        w_bc_lo[:, kt, bc * N:(bc + 1) * N], xT_hi[:, kt, t * TT:(t + 1) * TT],
                                        xT_lo[:, kt, t * TT:(t + 1) * TT], start=(kt == 0), stop=(kt == KT - 1))
                last.then_inc(bc_proj, 1)
            pe.wait_ge(dA_ready, 1)
            half = NC // 2
            for b in range(2):
                last = nc.tensor.matmul(bank(6 + b), upper[:], dA[:, b * half:(b + 1) * half, :], start=True, stop=True)
            last.then_inc(cum_psum, 1)
            for b in range(2):
                last = nc.tensor.matmul(bank(4 + b), ones[:], dA[:, b * half:(b + 1) * half, :], start=True, stop=True)
            last.then_inc(total_psum, 1)
            pe.wait_ge(end_arg_ready, 1)
            pe.wait_ge(decays_done, 3)
            for g in range(NT):
                for c in range(CPT):
                    last = nc.tensor.transpose(psum[0:H, 4 + g, c * CH:(c + 1) * CH], cum[:, g * CPT + c, :], ident[:])
                last.then_inc(cum_turned, 1)
            pe.wait_ge(bc_ready, 2)
            for g in range(NT):
                for c in range(CPT):
                    tok = (g * CPT + c) * CH
                    last = nc.tensor.transpose(bank(g)[:, c * N:(c + 1) * N], conv[:, 0, tok:tok + CH], ident[:])
                last.then_inc(B_turned, 1)
            for g in range(NT):
                pe.wait_ge(B_tok_done, g + 1)
                for c in range(CPT):
                    tok = (g * CPT + c) * CH
                    last = nc.tensor.matmul(bank(g)[:, c * CH:(c + 1) * CH], conv[:, 0, tok:tok + CH],
                                            CT[:, tok:tok + CH], start=True, stop=True)
                last.then_inc(CB_psum, 1)
    st.close()

    st, sb = scope()
    win_raw = sb("win_raw", [P, KT, 2, P], F32)
    win_hi = sb("win_hi", [P, KT, 2, P], F32R)
    win_lo = sb("win_lo", [P, KT, 2, P], F32R)
    wo_raw = sb("wo_raw", [P, D], F32)
    wo_norm = sb("wo_norm", [P, D], F32)
    wo_hi = sb("wo_hi", [P, 2, D], F32R)
    wo_lo = sb("wo_lo", [P, 2, D], F32R)
    x_raw = sb("x_raw", [P, TAPS - 1 + L], F32)
    xs = sb("xs", [P, 2, L], F32)
    sg = sb("sg", [P, 2, L], F32)
    xdt = sb("xdt", [P, 2, CPT, 2, HP], F32)
    xend = sb("xend", [P, 2, CPT, 2, HP], F32)
    cum_row = sb("cum_row", [P, 2, 2, TT], F32)
    M = sb("M", [P, 2, 2, TT], F32)
    state = sb("state", [P, 8, 2, HP], F32)
    zero_state = sb("zero_state", [P, 2, HP], F32)
    y = sb("y", [P, 2, CPT, 2, HP], F32)
    hid = sb("hid", [P, 2, TT], F32)
    hid_hi = sb("hid_hi", [P, 2, TT], F32R)
    hid_lo = sb("hid_lo", [P, 2, TT], F32R)
    sq = sb("sq", [P, TT], F32)
    row = sb("row", [P, 2, CONV_AT], F32)
    conv_row = sb("conv_row", [P, 2, TAPS + 1], F32)

    row_in = [sem("row_in0"), sem("row_in1")]
    conv_row_in = [sem("conv_row_in0"), sem("conv_row_in1")]
    names = ("pad_zero win_in win_hi_done win_lo_done wo_in wo_norm_done wo_hi_done wo_lo_done x_proj g_proj "
             "x_evac g_evac tap0_done conv_step conv_done xs_done sg_done x_turned xdt_done xend_done "
             "states_done scan_step diff_done decay_done M_done diag_done off_done y_off_done y_done y_turned v_done hid_done "
             "hid_hi_done hid_lo_done sq_done squares_done out_done mixed_done")
    (pad_zero, win_in, win_hi_done, win_lo_done, wo_in, wo_norm_done, wo_hi_done, wo_lo_done, x_proj, g_proj,
     x_evac, g_evac, tap0_done, conv_step, conv_done, xs_done, sg_done, x_turned, xdt_done, xend_done,
     states_done, scan_step, diff_done, decay_done, M_done, diag_done, off_done, y_off_done, y_done, y_turned, v_done, hid_done,
     hid_hi_done, hid_lo_done, sq_done, squares_done, out_done, mixed_done) = [sem(n) for n in names.split()]
    cum_in = [sem("cum_in0"), sem("cum_in1")]
    XB, GB, XT_BANK, ST_BANK, DIAG, OFF, YT_BANK, OUT = range(8)
    STEPS = 2 * (NC - 1)

    def wait(eng, semaphore, value):
        if not (isinstance(value, int) and value <= 0):
            eng.wait_ge(semaphore, value)

    def per_chunk_head(at, par, t):
        at += t * CPT * 2
        return row[:, par, at:at + CPT * 2].rearrange("p (c h) -> p c h", h=2).unsqueeze(3).to_broadcast([P, CPT, 2, HP])

    def rows_of(k, par):
        return k * 8 + (16 - 8 * par)

    def scalar_of(at, par, chunk=0, h=0):
        return row[:, par, at + 2 * chunk + h:at + 2 * chunk + h + 1]

    def tile(t):
        return slice(t * TT, (t + 1) * TT)

    def pairs(eng, body):
        body(0, 0, True, False)
        body(1, 1, False, False)
        with eng.Fori(1, PAIRS // 2 - 1) as i:
            body(i * 2, 0, False, False)
            body(i * 2 + 1, 1, False, False)
        body(PAIRS - 2, 0, False, False)
        body(PAIRS - 1, 1, False, True)

    def has_next2(k):
        return not (isinstance(k, int) and k + 2 >= PAIRS)

    with nc.Block() as block:
        @block.sync
        def _(sp):
            def at(value):
                return value if isinstance(value, int) else sp.snap(value)

            def load_win(k):
                x_at, g_at = at(k * P + X_COL), at(k * P)
                wait(sp, win_lo_done, k)
                wait(sp, win_hi_done, k)
                sp.dma_start(win_raw[:, :, 0, :], w_in_t[:, :, bass.ds(x_at, P)]).then_inc(win_in, 16)
                sp.dma_start(win_raw[:, :, 1, :], w_in_t[:, :, bass.ds(g_at, P)]).then_inc(win_in, 16)

            def load_wo(k):
                row = at(k * P)
                wait(sp, wo_norm_done, k)
                sp.dma_start(wo_raw[:], w_out[bass.ds(row, P), :]).then_inc(wo_in, 16)

            def load_cum(k, t):
                head = [at(k * 2), at(k * 2 + 1)]
                wait(sp, diff_done, 8 * k + 2 * t - 2)
                for h in range(2):
                    sp.dma_start(cum_row[:, t % 2, h, :],
                                 cum_dram[bass.ds(head[h], 1), tile(t)].partition_broadcast(P)
                                 .rearrange("p o t -> p (o t)")).then_inc(cum_in[t % 2], 16)

            def load_row(k, par):
                pair = at(k)
                wait(sp, v_done, 4 * k - 4)
                sp.dma_start(row[:, par, :], table_dram[:, bass.ds(pair, 1), HEAD:HEAD + CONV_AT]
                             .rearrange("p o r -> p (o r)")).then_inc(row_in[par], 16)

            def load_conv_row(k, par):
                pair = at(k)
                wait(sp, xs_done, 4 * k - 4)
                sp.dma_start(conv_row[:, par, :], table_dram[:, bass.ds(pair, 1), HEAD + CONV_AT:ROW]
                             .rearrange("p o r -> p (o r)")).then_inc(conv_row_in[par], 16)

            load_win(0)
            load_conv_row(0, 0)
            load_row(0, 0)
            load_wo(0)
            load_cum(0, 0)
            load_cum(0, 1)
            load_win(1)
            load_conv_row(1, 1)

            def body(k, par, first, last):
                if not last and not has_next2(k):
                    load_row(k + 1, 1 - par)
                if has_next2(k):
                    load_win(k + 2)
                    load_row(k + 1, 1 - par)
                    load_conv_row(k + 2, par)
                if not last:
                    load_wo(k + 1)
                load_cum(k, 2)
                load_cum(k, 3)
                if not last:
                    load_cum(k + 1, 0)
                    load_cum(k + 1, 1)

            pairs(sp, body)

        def win_split_hi(act, k):
            act.wait_ge(win_in, (k + 1) * 32)
            wait(act, g_proj, 4 * k)
            nc.scalar.activation(win_hi[:], win_raw[:], ACT.Copy).then_inc(win_hi_done, 1)

        def wo_split_hi(act, k, par):
            act.wait_ge(wo_norm_done, k + 1)
            wait(act, out_done, 8 * k - 8)
            nc.scalar.activation(wo_hi[:, par, :], wo_norm[:], ACT.Copy).then_inc(wo_hi_done, 1)

        @block.scalar
        def _(act):
            def evac_x(k, t):
                act.wait_ge(x_proj, 4 * k + t + 1)
                wait(act, conv_done, 4 * k)
                nc.scalar.activation(x_raw[:, TAPS - 1 + t * TT:TAPS - 1 + (t + 1) * TT], bank(XB),
                                     ACT.Copy).then_inc(x_evac, 1)

            def evac_g(k, par, t):
                act.wait_ge(g_proj, 4 * k + t + 1)
                wait(act, hid_done, 4 * k - 4)
                nc.scalar.activation(sg[:, par, tile(t)], bank(GB), ACT.Copy).then_inc(g_evac, 1)

            def decays(k, par, t, h):
                act.wait_ge(diff_done, 8 * k + 2 * t + h + 1)
                nc.scalar.activation(M[:, t % 2, h, :], M[:, t % 2, h, :], ACT.Exp).then_inc(decay_done, 1)

            def split_hid(k, t):
                act.wait_ge(hid_done, 4 * k + t + 1)
                wait(act, out_done, 8 * k + 2 * t - 2)
                nc.scalar.activation(hid_hi[:, t % 2, :], hid[:, t % 2, :], ACT.Copy).then_inc(hid_hi_done, 1)

            def square(k, t):
                wait(act, squares_done, 4 * k + t)
                nc.scalar.activation(sq[:], hid[:, t % 2, :], ACT.Square).then_inc(sq_done, 1)

            def silus(k, par):
                for t in range(NT):
                    act.wait_ge(conv_done, 4 * k + t + 1)
                    nc.scalar.activation(xs[:, par, tile(t)], xs[:, par, tile(t)], ACT.Silu,
                                         bias=conv_row[:, par, TAPS:TAPS + 1]).then_inc(xs_done, 1)
                act.wait_ge(g_evac, 4 * k + 4)
                for t in range(NT):
                    nc.scalar.activation(sg[:, par, tile(t)], sg[:, par, tile(t)], ACT.Silu).then_inc(sg_done, 1)

            win_split_hi(act, 0)
            for t in range(NT):
                evac_x(0, t)
                evac_g(0, 0, t)
            silus(0, 0)
            wo_split_hi(act, 0, 0)
            win_split_hi(act, 1)
            decays(0, 0, 0, 0)
            decays(0, 0, 0, 1)

            def body(k, par, first, last):
                n, npar = k + 1, 1 - par
                if not last:
                    evac_x(n, 0)
                if not first:
                    split_hid(k - 1, 3)
                decays(k, par, 1, 0)
                if not last:
                    evac_x(n, 1)
                if not first:
                    square(k - 1, 3)
                decays(k, par, 1, 1)
                if not last:
                    evac_g(n, npar, 0)
                    evac_x(n, 2)
                split_hid(k, 0)
                decays(k, par, 2, 0)
                if not last:
                    evac_x(n, 3)
                square(k, 0)
                decays(k, par, 2, 1)
                if not last:
                    evac_g(n, npar, 1)
                    evac_g(n, npar, 2)
                split_hid(k, 1)
                decays(k, par, 3, 0)
                if not last:
                    evac_g(n, npar, 3)
                square(k, 1)
                decays(k, par, 3, 1)
                split_hid(k, 2)
                square(k, 2)
                if not last:
                    silus(n, npar)
                    wo_split_hi(act, n, npar)
                    if has_next2(k):
                        win_split_hi(act, k + 2)
                    decays(n, npar, 0, 0)
                    decays(n, npar, 0, 1)

            pairs(act, body)
            split_hid(PAIRS - 1, 3)
            square(PAIRS - 1, 3)

        @block.gpsimd
        def _(pool):
            nc.gpsimd.memset(x_raw[:, 0:TAPS - 1], 0.0).then_inc(pad_zero, 1)
            nc.gpsimd.memset(zero_state[:], 0.0).then_inc(pad_zero, 1)

            def tap0(k, par, t):
                wait(pool, v_done, 4 * k - 4)
                pool.wait_ge(x_evac, 4 * k + t + 1)
                pool.wait_ge(conv_row_in[par], rows_of(k, par))
                nc.gpsimd.tensor_tensor(xs[:, par, tile(t)], x_raw[:, tile(t)],
                                        conv_row[:, par, 0:1].to_broadcast([P, TT]), ALU.mult).then_inc(tap0_done, 1)

            def to_chunk_end(k, par, t):
                pool.wait_ge(xdt_done, 4 * k + t + 1)
                wait(pool, states_done, 4 * k + t - 1)
                nc.gpsimd.tensor_tensor(xend[:, t % 2], xdt[:, t % 2], per_chunk_head(TO_END, par, t),
                                        ALU.mult).then_inc(xend_done, 1)

            def gate(k, par, t):
                pool.wait_ge(v_done, 4 * k + t + 1)
                pool.wait_ge(sg_done, 4 * k + t + 1)
                nc.gpsimd.tensor_tensor(hid[:, t % 2, :], hid[:, t % 2, :], sg[:, par, tile(t)],
                                        ALU.mult).then_inc(hid_done, 1)

            def split_hid(k, t):
                pool.wait_ge(hid_hi_done, 4 * k + t + 1)
                nc.gpsimd.tensor_tensor(hid_lo[:, t % 2, :], hid[:, t % 2, :], hid_hi[:, t % 2, :].bitcast(F32),
                                        ALU.subtract).then_inc(hid_lo_done, 1)

            def add_squares(k, t):
                pool.wait_ge(sq_done, 4 * k + t + 1)
                nc.gpsimd.tensor_tensor(squares[:, tile(t)], squares[:, tile(t)], sq[:], ALU.add).then_inc(squares_done, 1)

            def win_split_lo(k):
                pool.wait_ge(win_hi_done, k + 1)
                nc.gpsimd.tensor_tensor(win_lo[:], win_raw[:], win_hi[:].bitcast(F32),
                                        ALU.subtract).then_inc(win_lo_done, 1)

            def wo_split_lo(k, par):
                pool.wait_ge(wo_hi_done, k + 1)
                nc.gpsimd.tensor_tensor(wo_lo[:, par, :], wo_norm[:], wo_hi[:, par, :].bitcast(F32),
                                        ALU.subtract).then_inc(wo_lo_done, 1)

            win_split_lo(0)
            pool.wait_ge(pad_zero, 2)
            for t in range(NT):
                tap0(0, 0, t)
            wo_split_lo(0, 0)
            win_split_lo(1)
            to_chunk_end(0, 0, 0)

            def body(k, par, first, last):
                n, npar = k + 1, 1 - par
                if not last:
                    tap0(n, npar, 0)
                if not first:
                    gate(k - 1, npar, 3)
                to_chunk_end(k, par, 1)
                if not first:
                    split_hid(k - 1, 3)
                if not last:
                    tap0(n, npar, 1)
                if not first:
                    add_squares(k - 1, 3)
                if not last:
                    tap0(n, npar, 2)
                gate(k, par, 0)
                to_chunk_end(k, par, 2)
                split_hid(k, 0)
                if not last:
                    tap0(n, npar, 3)
                add_squares(k, 0)
                gate(k, par, 1)
                to_chunk_end(k, par, 3)
                split_hid(k, 1)
                add_squares(k, 1)
                gate(k, par, 2)
                split_hid(k, 2)
                add_squares(k, 2)
                if not last:
                    wo_split_lo(n, npar)
                    if has_next2(k):
                        win_split_lo(k + 2)
                    to_chunk_end(n, npar, 0)

            pairs(pool, body)
            gate(PAIRS - 1, 1, 3)
            split_hid(PAIRS - 1, 3)
            add_squares(PAIRS - 1, 3)

        @block.vector
        def _(dve):
            def conv_tap(k, par, t, tap):
                if tap == 1:
                    dve.wait_ge(tap0_done, 4 * k + t + 1)
                else:
                    dve.wait_ge(conv_step, (4 * k + t) * 2 + tap - 1)
                ins = nc.vector.scalar_tensor_tensor(xs[:, par, tile(t)], x_raw[:, t * TT + tap:(t + 1) * TT + tap],
                                                     conv_row[:, par, tap:tap + 1], xs[:, par, tile(t)],
                                                     ALU.mult, ALU.add)
                ins.then_inc(conv_done if tap == TAPS - 1 else conv_step, 1)

            def times_dt(k, par, t):
                dve.wait_ge(row_in[par], rows_of(k, par))
                dve.wait_ge(x_turned, 4 * k + t + 1)
                wait(dve, diag_done, 4 * k + t - 1)
                wait(dve, xend_done, 4 * k + t - 1)
                nc.vector.tensor_tensor(xdt[:, t % 2], bank(XT_BANK).rearrange("p (c h q) -> p c h q", h=2, q=HP),
                                        per_chunk_head(DT, par, t), ALU.mult).then_inc(xdt_done, 1)

            def diffs(k, par, t, h):
                dve.wait_ge(cum_in[t % 2], (2 * k + t // 2 + 1) * 32)
                dve.wait_ge(row_in[par], rows_of(k, par))
                wait(dve, diag_done, 4 * k + t - 1)
                for c in range(CPT):
                    cum_j = scalar_of(CUM, par, t * CPT + c, h)
                    last = nc.vector.tensor_scalar(M[:, t % 2, h, c * CH:(c + 1) * CH],
                                                   cum_row[:, t % 2, h, c * CH:(c + 1) * CH], cum_j, cum_j,
                                                   ALU.min, ALU.subtract)
                last.then_inc(diff_done, 1)

            def masked(k, t):
                dve.wait_ge(decay_done, 8 * k + 2 * t + 2)
                cb = CB[:, t * CPT:(t + 1) * CPT, :].rearrange("p c i -> p (c i)").unsqueeze(1).to_broadcast([P, 2, TT])
                nc.vector.tensor_tensor(M[:, t % 2], M[:, t % 2], cb, ALU.mult).then_inc(M_done, 1)

            def scan(k, par, t):
                dve.wait_ge(states_done, 4 * k + t + 1)
                wait(dve, off_done, 4 * k + t - 1)
                for c in range(CPT):
                    chunk = t * CPT + c
                    if chunk == NC - 1:
                        continue
                    if c == CPT - 1:
                        wait(dve, off_done, 4 * k + t)
                    for h in range(2):
                        step = 2 * chunk + h
                        wait(dve, scan_step, STEPS * k + step - 1)
                        before = zero_state[:, h, :] if chunk == 0 else state[:, chunk % 8, h, :]
                        nc.vector.scalar_tensor_tensor(
                            state[:, (chunk + 1) % 8, h, :], before,
                            scalar_of(CHUNK_DECAY, par, chunk, h),
                            bank(ST_BANK)[:, c * P + h * HP:c * P + (h + 1) * HP],
                            ALU.mult, ALU.add).then_inc(scan_step, 1)

            def scale_off(k, par, t):
                dve.wait_ge(off_done, 4 * k + t + 1)
                wait(dve, y_turned, 4 * k + t - 1)
                nc.vector.tensor_tensor(y[:, t % 2], bank(OFF).rearrange("p (c h q) -> p c h q", h=2, q=HP),
                                        per_chunk_head(E_CUM, par, t), ALU.mult).then_inc(y_off_done, 1)

            def add_diag(k, t):
                dve.wait_ge(diag_done, 4 * k + t + 1)
                dve.wait_ge(y_off_done, 4 * k + t + 1)
                yt = y[:, t % 2].rearrange("p c h q -> p (c h q)")
                nc.vector.tensor_tensor(yt, bank(DIAG), yt, ALU.add).then_inc(y_done, 1)

            def skip_path(k, par, t):
                dve.wait_ge(y_turned, 4 * k + t + 1)
                wait(dve, hid_lo_done, 4 * k + t - 1)
                wait(dve, sq_done, 4 * k + t - 1)
                nc.vector.scalar_tensor_tensor(hid[:, t % 2, :], xs[:, par, tile(t)], scalar_of(D_AT, par),
                                               bank(YT_BANK), ALU.mult, ALU.add).then_inc(v_done, 1)

            def add_out(k, t, m):
                dve.wait_ge(out_done, 8 * k + 2 * t + m + 1)
                nc.vector.tensor_tensor(mixed[:, m, tile(t)], bank(OUT), mixed[:, m, tile(t)],
                                        ALU.add).then_inc(mixed_done, 1)

            def wo_scale(k, par):
                dve.wait_ge(row_in[par], rows_of(k, par))
                dve.wait_ge(wo_in, (k + 1) * 16)
                wait(dve, wo_lo_done, k)
                nc.vector.tensor_scalar(wo_norm[:], wo_raw[:], scalar_of(NORM_AT, par), None,
                                        ALU.mult).then_inc(wo_norm_done, 1)

            diffs(0, 0, 0, 0)
            diffs(0, 0, 0, 1)
            dve.wait_ge(pad_zero, 2)
            for t in range(NT):
                for tap in range(1, TAPS):
                    conv_tap(0, 0, t, tap)
            wo_scale(0, 0)
            times_dt(0, 0, 0)
            masked(0, 0)
            scan(0, 0, 0)

            def body(k, par, first, last):
                n, npar = k + 1, 1 - par
                tap = (lambda t, j: None) if last else (lambda t, j: conv_tap(n, npar, t, j))
                if not first:
                    add_out(k - 1, 2, 1)
                    skip_path(k - 1, npar, 3)
                times_dt(k, par, 1)
                diffs(k, par, 1, 0)
                diffs(k, par, 1, 1)
                tap(0, 1)
                scale_off(k, par, 0)
                tap(0, 2)
                add_diag(k, 0)
                tap(0, 3)
                masked(k, 1)
                tap(1, 1)
                scan(k, par, 1)
                tap(1, 2)
                if not first:
                    add_out(k - 1, 3, 0)
                tap(1, 3)
                if not first:
                    add_out(k - 1, 3, 1)
                skip_path(k, par, 0)
                times_dt(k, par, 2)
                diffs(k, par, 2, 0)
                diffs(k, par, 2, 1)
                tap(2, 1)
                scale_off(k, par, 1)
                tap(2, 2)
                add_diag(k, 1)
                tap(2, 3)
                masked(k, 2)
                tap(3, 1)
                scan(k, par, 2)
                tap(3, 2)
                add_out(k, 0, 0)
                tap(3, 3)
                add_out(k, 0, 1)
                skip_path(k, par, 1)
                times_dt(k, par, 3)
                diffs(k, par, 3, 0)
                diffs(k, par, 3, 1)
                scale_off(k, par, 2)
                if not last:
                    wo_scale(n, npar)
                add_diag(k, 2)
                masked(k, 3)
                scan(k, par, 3)
                add_out(k, 1, 0)
                add_out(k, 1, 1)
                skip_path(k, par, 2)
                if not last:
                    diffs(n, npar, 0, 0)
                    diffs(n, npar, 0, 1)
                scale_off(k, par, 3)
                add_diag(k, 3)
                add_out(k, 2, 0)
                if not last:
                    times_dt(n, npar, 0)
                    masked(n, 0)
                    scan(n, npar, 0)

            pairs(dve, body)
            add_out(PAIRS - 1, 2, 1)
            skip_path(PAIRS - 1, 1, 3)
            add_out(PAIRS - 1, 3, 0)
            add_out(PAIRS - 1, 3, 1)

        @block.tensor
        def _(pe):
            def proj(k, par, which, t):
                b, done, evac = ((XB, x_proj, x_evac), (GB, g_proj, g_evac))[which]
                pe.wait_ge(win_lo_done, k + 1)
                wait(pe, evac, 4 * k + t)
                for kt in range(KT):
                    last = split_matmul(nc, bank(b), win_hi[:, kt, which, :], win_lo[:, kt, which, :],
                                        xT_hi[:, kt, tile(t)], xT_lo[:, kt, tile(t)],
                                        start=(kt == 0), stop=(kt == KT - 1))
                last.then_inc(done, 1)

            def turn_x(k, par, t):
                pe.wait_ge(xs_done, 4 * k + t + 1)
                wait(pe, xdt_done, 4 * k + t)
                for c in range(CPT):
                    tok = t * TT + c * CH
                    last = nc.tensor.transpose(bank(XT_BANK)[:, c * P:(c + 1) * P], xs[:, par, tok:tok + CH], ident[:])
                last.then_inc(x_turned, 1)

            def states(k, t):
                pe.wait_ge(xend_done, 4 * k + t + 1)
                wait(pe, scan_step, STEPS * k + 8 * t)
                for c in range(CPT):
                    last = nc.tensor.matmul(bank(ST_BANK)[:, c * P:(c + 1) * P], B_tok[:, t * CPT + c, :],
                                            xend[:, t % 2, c].rearrange("p h q -> p (h q)"), start=True, stop=True)
                last.then_inc(states_done, 1)

            def diag(k, t):
                pe.wait_ge(M_done, 4 * k + t + 1)
                wait(pe, y_done, 4 * k + t)
                for c in range(CPT):
                    for h in range(2):
                        last = nc.tensor.matmul(bank(DIAG)[:, c * P + h * HP:c * P + (h + 1) * HP],
                                                M[:, t % 2, h, c * CH:(c + 1) * CH], xdt[:, t % 2, c, h, :],
                                                start=True, stop=True)
                last.then_inc(diag_done, 1)

            def off(k, t):
                pe.wait_ge(scan_step, STEPS * k + 8 * t + 6)
                wait(pe, y_off_done, 4 * k + t)
                for c in range(CPT):
                    chunk = t * CPT + c
                    before = zero_state[:] if chunk == 0 else state[:, chunk % 8]
                    last = nc.tensor.matmul(bank(OFF)[:, c * P:(c + 1) * P], CT[:, chunk * CH:(chunk + 1) * CH],
                                            before.rearrange("p h q -> p (h q)"), start=True, stop=True)
                last.then_inc(off_done, 1)

            def turn_y(k, t):
                pe.wait_ge(y_done, 4 * k + t + 1)
                wait(pe, v_done, 4 * k + t)
                for c in range(CPT):
                    last = nc.tensor.transpose(bank(YT_BANK)[:, c * CH:(c + 1) * CH],
                                               y[:, t % 2, c].rearrange("p h q -> p (h q)"), ident[:])
                last.then_inc(y_turned, 1)

            def out_proj(k, par, t, m):
                pe.wait_ge(hid_lo_done, 4 * k + t + 1)
                pe.wait_ge(wo_lo_done, k + 1)
                wait(pe, mixed_done, 8 * k + 2 * t + m)
                split_matmul(nc, bank(OUT), wo_hi[:, par, m * P:(m + 1) * P], wo_lo[:, par, m * P:(m + 1) * P],
                             hid_hi[:, t % 2, :], hid_lo[:, t % 2, :], start=True, stop=True).then_inc(out_done, 1)

            for t in range(NT):
                proj(0, 0, 0, t)
                proj(0, 0, 1, t)
            turn_x(0, 0, 0)
            states(0, 0)

            def body(k, par, first, last):
                n, npar = k + 1, 1 - par
                x_of = (lambda t: None) if last else (lambda t: proj(n, npar, 0, t))
                g_of = (lambda t: None) if last else (lambda t: proj(n, npar, 1, t))
                turn_x(k, par, 1)
                x_of(0)
                off(k, 0)
                diag(k, 0)
                x_of(1)
                states(k, 1)
                g_of(0)
                if not first:
                    out_proj(k - 1, npar, 3, 0)
                turn_y(k, 0)
                if not first:
                    out_proj(k - 1, npar, 3, 1)
                turn_x(k, par, 2)
                x_of(2)
                off(k, 1)
                diag(k, 1)
                x_of(3)
                states(k, 2)
                g_of(1)
                out_proj(k, par, 0, 0)
                turn_y(k, 1)
                out_proj(k, par, 0, 1)
                turn_x(k, par, 3)
                g_of(2)
                off(k, 2)
                diag(k, 2)
                g_of(3)
                states(k, 3)
                out_proj(k, par, 1, 0)
                turn_y(k, 2)
                out_proj(k, par, 1, 1)
                off(k, 3)
                diag(k, 3)
                out_proj(k, par, 2, 0)
                if not last:
                    turn_x(n, npar, 0)
                turn_y(k, 3)
                out_proj(k, par, 2, 1)
                if not last:
                    states(n, 0)

            pairs(pe, body)
            out_proj(PAIRS - 1, 1, 3, 0)
            out_proj(PAIRS - 1, 1, 3, 1)
    st.close()
    shared_scope.close()

    st, sb = scope()
    x_res = sb("x_res3", [P, NC, D], F32)
    xn = sb("xn3", [P, NC, D], F32)
    w = {n + part: sb(n + part + "3", shape, F32R)
         for n, shape in ffn_w_shapes.items() for part in ("_hi", "_lo")}
    rms_ve = sb("rms_ve", [P, NC], F32)
    rms_sd = sb("rms_sd", [P, NC], F32)
    rms_t = sb("rms_t", [P, NC], F32)
    rms = sb("rms", [P, NC], F32)
    ln3 = LayerNorm(nc, "ln3", sem, sb, x_res, xn, xT_hi, xT_lo, [(bank(6), bank(7)), (bank(4), bank(5))], ident)
    ffn2 = Ffn(nc, "ffn2", sem, sb, bank, x_res, xT_hi, xT_lo, w)
    x1_in, w_back = sem("x1_in"), sem("w_back")
    sums_psum, rms_var, rms_sd_ready, rms_step = sem("sums_psum"), sem("rms_var"), sem("rms_sd_ready"), sem("rms_step")
    mixed_turned, x2_done, rows_out = sem("mixed_turned"), sem("x2_done"), sem("rows_out")

    with nc.Block() as block:
        @block.sync
        def _(sp):
            sp.dma_start(x_res[:], x1_dram).then_inc(x1_in, 16)
            for n in ORDER:
                for part in ("_hi", "_lo"):
                    sp.dma_start(w[n + part][:].bitcast(F32), w_dram[n + part]).then_inc(w_back, 16)
            for T in range(NT):
                sp.wait_ge(ffn2.x_done, T + 2)
                sp.dma_start(out_rows[:, T * CPT:(T + 1) * CPT, :],
                             x_res[:, T * CPT:(T + 1) * CPT, :]).then_inc(rows_out, 16)
            sp.wait_ge(rows_out, 16 * NT)

        @block.gpsimd
        def _(pool):
            ffn2.pool(pool)

        @block.scalar
        def _(act):
            act.wait_ge(rms_var, 1)
            nc.scalar.activation(rms_sd[:], rms_ve[:], ACT.Sqrt).then_inc(rms_sd_ready, 1)
            ln3.scalar_sqrt(act)
            ln3.scalar_hi(act)
            ffn2.scalar(act)

        @block.vector
        def _(dve):
            steps = [0]

            def chain(dve, ins):
                steps[0] += 1
                ins.then_inc(rms_step, 1)
                dve.wait_ge(rms_step, steps[0])

            dve.wait_ge(sums_psum, 1)
            nc.vector.tensor_scalar(rms_ve[:], bank(0)[:, 0:NC], 1.0 / DI, EPS, ALU.mult, ALU.add).then_inc(rms_var, 1)
            rsqrt_from_sqrt(nc, dve, rms_sd, rms_ve, rms, rms_t, rms_sd_ready, chain)
            dve.wait_ge(x1_in, 16)
            for s in range(NC):
                dve.wait_ge(mixed_turned, s + 1)
                nc.vector.scalar_tensor_tensor(x_res[:, s, :], bank(1 + s % 3)[:, 0:D], rms[:, s:s + 1], x_res[:, s, :],
                                               ALU.mult, ALU.add).then_inc(x2_done, 1)
                if s >= 1:
                    dve.wait_ge(x2_done, s)
                    ln3.stats_of(s - 1)
            dve.wait_ge(x2_done, NC)
            ln3.stats_of(NC - 1)
            ln3.vector_stats(dve)
            ln3.vector_normalise(dve)
            ln3.vector_lo(dve)
            ffn2.vector(dve)

        @block.tensor
        def _(pe):
            for c in range(NC):
                last = nc.tensor.matmul(bank(0)[:, c:c + 1], squares[:, c * CH:(c + 1) * CH], ones[:, 0:1],
                                        start=True, stop=True)
            last.then_inc(sums_psum, 1)
            for s in range(NC):
                if s >= 3:
                    pe.wait_ge(x2_done, s - 2)
                for m in range(KT):
                    last = nc.tensor.transpose(bank(1 + s % 3)[:, m * P:(m + 1) * P], mixed[:, m, s * CH:(s + 1) * CH],
                                               ident[:])
                last.then_inc(mixed_turned, 1)
            ln3.tensor_transpose(pe)
            ffn2.tensor(pe, lambda: pe.wait_ge(w_back, 16 * 2 * len(ORDER)))
    st.close()
    acc_scope.close()
    whole.close()
    ctx.close()


INPUTS = ["L0_attn_hidden_states", "L0_attn_in_proj_w", "L0_attn_conv_w", "L0_attn_conv_b", "L0_attn_dt_bias",
          "L0_attn_A_log", "L0_attn_D_param", "L0_attn_norm_w", "L0_attn_out_proj_w", "L0_ffn_lut",
          "L0_ffn_gate_idx", "L0_ffn_up_idx", "L0_ffn_down_idx"]


def kernel(**inputs):
    import numpy as np
    import concourse.bacc as bacc
    from concourse.bass_utils import run_bass_kernel_spmd

    nc = bacc.Bacc("TRN2", target_bir_lowering=False, num_devices=1)
    arrays, args = {}, []
    for name in INPUTS:
        a = np.ascontiguousarray(inputs[name])
        arrays[name + "_dram"] = a
        args.append(nc.dram_tensor(name + "_dram", a.shape, mybir.dt.from_np(a.dtype), kind="ExternalInput").ap())
    out = nc.dram_tensor("out_dram", (1, L, D), F32, kind="ExternalOutput").ap()
    macaron(nc, *args, out)
    result = run_bass_kernel_spmd(nc, [arrays], core_ids=[0])
    return result.results[0]["out_dram"]
```
